# Optimizing a Trainium2 kernel written in Bass

```python
import numpy as np
import jax
import jax.numpy as jnp

def _softmax(x, axis=-1):
    return jax.nn.softmax(x, axis=axis)
def _gelu(x):
    return jax.nn.gelu(x, approximate=True)
def _silu(x):
    return jax.nn.silu(x)
def _sigmoid(x):
    return jax.nn.sigmoid(x)
def _layernorm(x, axis=-1, eps=1e-5):
    m = jnp.mean(x, axis=axis, keepdims=True)
    v = jnp.var(x, axis=axis, keepdims=True)
    return (x - m) / jnp.sqrt(v + eps)
def _scatter_add(tgt, idx, src, axis=0):
    return tgt.at[idx].add(src)
def _segment_sum(src, seg, n):
    return jax.ops.segment_sum(src, seg, n)

kernel_name = 'mk_conv_preact_d1_conv_nhwc32_d18857'

def setup_inputs(seed: int = 0):
    np.random.seed(seed)
    _w = jnp.asarray
    def _rec_inputs():
        import jax
        import jax.numpy as jnp
        _gk = jax.random.key(seed)
        x = 7.22e-05 + 1 * jax.random.normal(jax.random.fold_in(_gk, 1), (32, 256, 32, 32), jnp.float32)
        return x
    x = _rec_inputs()
    def _L0_conv_setup():
        import jax, jax.numpy as jnp
        import numpy as np
        B, C, W, H = (32, 256, 32, 32)
        key = jax.random.key(seed)
        ks = jax.random.split(key, 9)
        s = 1.0 / np.sqrt(C)
        return {'x': jax.random.normal(ks[0], (B, C, W, H), dtype=jnp.float32), 'Wq': jax.random.normal(ks[1], (C, C), dtype=jnp.float32) * s, 'bq': jax.random.normal(ks[2], (C,), dtype=jnp.float32) * 0.01, 'Wk': jax.random.normal(ks[3], (C, C), dtype=jnp.float32) * s, 'bk': jax.random.normal(ks[4], (C,), dtype=jnp.float32) * 0.01, 'Wv': jax.random.normal(ks[5], (C, C), dtype=jnp.float32) * s, 'bv': jax.random.normal(ks[6], (C,), dtype=jnp.float32) * 0.01, 'rel_h': jax.random.normal(ks[7], (1, C, 1, H), dtype=jnp.float32), 'rel_w': jax.random.normal(ks[8], (1, C, W, 1), dtype=jnp.float32)}
    _L0_conv_all = _L0_conv_setup()
    _L0_conv_in = {k: v for k, v in _L0_conv_all.items() if k in ('Wq', 'bq', 'Wk', 'bk', 'Wv', 'bv', 'rel_h', 'rel_w', )}
    del _L0_conv_all

    return {
        "x": x,
        "L0_conv_Wq": _L0_conv_in["Wq"],
        "L0_conv_bq": _L0_conv_in["bq"],
        "L0_conv_Wk": _L0_conv_in["Wk"],
        "L0_conv_bk": _L0_conv_in["bk"],
        "L0_conv_Wv": _L0_conv_in["Wv"],
        "L0_conv_bv": _L0_conv_in["bv"],
        "L0_conv_rel_h": _L0_conv_in["rel_h"],
        "L0_conv_rel_w": _L0_conv_in["rel_w"],
    }

def reference(x, L0_conv_Wq, L0_conv_bq, L0_conv_Wk, L0_conv_bk, L0_conv_Wv, L0_conv_bv, L0_conv_rel_h, L0_conv_rel_w):
    import jax
    import jax.numpy as jnp
    def _L0_conv_ref(x, Wq, bq, Wk, bk, Wv, bv, rel_h, rel_w):
        import jax, jax.numpy as jnp
        import numpy as np
        B, C, W, H = (32, 256, 32, 32)
        b, c, w, h = x.shape
        n = w * h
        xf = x.reshape(b, c, n)
        q = jnp.einsum('oc,bcn->bon', Wq, xf) + bq[None, :, None]
        k = jnp.einsum('oc,bcn->bon', Wk, xf) + bk[None, :, None]
        v = jnp.einsum('oc,bcn->bon', Wv, xf) + bv[None, :, None]
        content_content = jnp.einsum('bci,bcj->bij', q, k)
        rel = (rel_h + rel_w).reshape(c, n)
        content_position = jnp.einsum('cp,bcj->bpj', rel, q)
        attention = jax.nn.softmax(content_content + content_position, axis=-1)
        out = jnp.einsum('bcj,bij->bci', v, attention)
        return out.reshape(b, c, w, h)

    def _gn(v, G=16, eps=1e-5):
        B_, H_, W_, C_ = v.shape
        g = v.reshape(B_, H_, W_, G, C_ // G)
        m = jnp.mean(g, axis=(1, 2, 4), keepdims=True)
        s = jnp.var(g, axis=(1, 2, 4), keepdims=True)
        return ((g - m) / jnp.sqrt(s + eps)).reshape(v.shape)

    def _ln_c(v, eps=1e-6):
        m = jnp.mean(v, axis=-1, keepdims=True)
        s = jnp.var(v, axis=-1, keepdims=True)
        return (v - m) / jnp.sqrt(s + eps)

    def _ln_t(v, eps=1e-5):
        m = jnp.mean(v, axis=-1, keepdims=True)
        s = jnp.var(v, axis=-1, keepdims=True)
        return (v - m) / jnp.sqrt(s + eps)

    def _to_tokens(v):
        B_, H_, W_, C_ = v.shape
        return v.reshape(B_, H_ * W_, C_)
    def _from_tokens(t, like):
        return t.reshape(like.shape)

    x = x + _L0_conv_ref(_gn(x), L0_conv_Wq, L0_conv_bq, L0_conv_Wk, L0_conv_bk, L0_conv_Wv, L0_conv_bv, L0_conv_rel_h, L0_conv_rel_w)
    return x


_drawn_inputs = setup_inputs


def setup_inputs(seed=0):
    import zlib

    import numpy as np

    out = dict(_drawn_inputs(seed))
    spreads = {}
    factors = {'L0_conv_bk': 8.0, 'L0_conv_bv': 7.532}
    for name, (base, spread) in spreads.items():
        noise = np.random.default_rng([zlib.crc32(name.encode()), seed]).standard_normal(out[name].shape)
        drawn = base * np.exp(spread * noise) if base else spread * noise
        out[name] = jnp.asarray(drawn.astype(out[name].dtype))
    for name, factor in factors.items():
        out[name] = (out[name] * factor).astype(out[name].dtype)
    return out
```

```python
from contextlib import ExitStack

import concourse.bass as bass
from concourse import mybir

F32 = mybir.dt.float32
F32R = mybir.dt.float32r
ALU = mybir.AluOpType
ACT = mybir.ActivationFunctionType
AX = mybir.AxisListType

P = 128
GROUPS = 16
EPS = 1e-5
STEPS = 8
SLOTS = {0: [("u", 2)], 1: [("u", 3), ("mean", 0), ("v", 0)], 2: [("v", 1)], 3: [("v", 2), ("var", 0)],
         4: [("v", 3)], 5: [("u", 0)], 6: [("u", 1)], 7: []}
NEXT = [("mean", 0), ("var", 0), ("u", 0), ("u", 1)]
STAGE = [use for s in range(STEPS) for use in [("turn", s, 0), ("turn", s, 1), *SLOTS[s]]]
STAGE_LAST = [use for use in STAGE if use not in NEXT]
PER_BATCH = len(STAGE)


def stage_use(b, use, last=False):
    order = STAGE_LAST if last else STAGE
    return b * PER_BATCH + len(NEXT) - 2 + order.index(use)


def attention_block(nc, x, w_q, b_q, w_k, w_v, b_v, rel_h, rel_w, out):
    B, C, W, H = x.shape
    N = W * H
    KC = C // P
    T = N // P
    HALF = N // 2
    TH = T // 2
    Q = P * 4
    WEIGHT_LOADS = 5 + 2 * KC
    COUNT = C * W * H // GROUPS
    assert KC == 2 and T == STEPS and HALF == Q and B % 2 == 0 and PER_BATCH % 2 == 0

    x_dram = x.rearrange("b (k p) w h -> b p k (w h)", p=P)
    out_dram = out.rearrange("b (k p) w h -> b p k (w h)", p=P)

    with ExitStack() as ctx:
        def sb(name, shape, dt=F32):
            return ctx.enter_context(nc.sbuf_tensor(name, shape, dt))

        def sem(name):
            return ctx.enter_context(nc.semaphore(name))

        z_hi = sb("z_hi", [P, 2, KC, N], F32R)
        z_lo = sb("z_lo", [P, 2, KC, N], F32R)
        u_hi = sb("u_hi", [P, KC, N], F32R)
        u_lo = sb("u_lo", [P, KC, N], F32R)
        v_hi = sb("v_hi", [P, T, C], F32R)
        v_lo = sb("v_lo", [P, T, C], F32R)
        pt_hi = sb("pt_hi", [P, 2, T, HALF], F32R)
        pt_lo = sb("pt_lo", [P, 2, T, HALF], F32R)
        at_hi = sb("at_hi", [P, KC, C], F32R)
        at_lo = sb("at_lo", [P, KC, C], F32R)
        wvt_hi = sb("wvt_hi", [P, KC, C], F32R)
        wvt_lo = sb("wvt_lo", [P, KC, C], F32R)
        front = sb("front", [P, KC, N])
        squares = sb("squares", [P, KC, N])
        resid = sb("resid", [P, 2, KC, HALF])
        probs = sb("probs", [P, 2, N])
        u_sum = sb("u_sum", [P, 2, HALF])
        r_bias = sb("r_bias", [P, KC, N])
        wq_sb = sb("wq_sb", [P, KC, C])
        wk_sb = sb("wk_sb", [P, KC, C])
        wv_sb = sb("wv_sb", [P, KC, C])
        bq_sb = sb("bq_sb", [P, KC])
        bv_sb = sb("bv_sb", [P, KC])
        relh_sb = sb("relh_sb", [P, KC, H])
        relw_sb = sb("relw_sb", [P, KC, W])
        kb_sb = sb("kb_sb", [P, KC])
        ident = sb("ident", [P, P])
        share = sb("share", [P, P])
        power = sb("power", [P, GROUPS])
        part = sb("part", [P, 2, GROUPS])
        mean = sb("mean", [P, GROUPS])
        var_eps = sb("var_eps", [P, GROUPS])
        rstd = sb("rstd", [P, GROUPS])
        neg_max = sb("neg_max", [P, 2])
        row_sum = sb("row_sum", [P, 2])
        row_inv = sb("row_inv", [P, 2])
        rel_sb = probs

        scores = [ctx.enter_context(nc.psum_tensor(f"scores{i}", [P, N], F32)) for i in range(2)]
        sums = ctx.enter_context(nc.psum_tensor("sums", [P, KC, HALF], F32))
        stage = [ctx.enter_context(nc.psum_tensor(f"stage{i}", [P, Q], F32)) for i in range(2)]

        weights_in = sem("weights_in")
        x_in = sem("x_in")
        resid_in = [sem(f"resid_in{h}") for h in range(2)]
        stored = [sem(f"stored{h}") for h in range(2)]
        const_ready = sem("const_ready")
        rel_ready = sem("rel_ready")
        prep_mm = sem("prep_mm")
        prep_hi = sem("prep_hi")
        prep_read = sem("prep_read")
        sum_done = sem("sum_done")
        sumsq_done = sem("sumsq_done")
        stat_mm = sem("stat_mm")
        centred_dve = sem("centred_dve")
        centred_pool = sem("centred_pool")
        squared = sem("squared")
        rstd_done = sem("rstd_done")
        z_scaled = sem("z_scaled")
        z_hi_done = sem("z_hi_done")
        z_lo_dve = sem("z_lo_dve")
        z_lo_pool = sem("z_lo_pool")
        u_mm = sem("u_mm")
        u_hi_done = sem("u_hi_done")
        u_ready = sem("u_ready")
        v_mm = sem("v_mm")
        v_hi_done = sem("v_hi_done")
        scores_ready = sem("scores_ready")
        max_done = sem("max_done")
        exp_done = sem("exp_done")
        inv_done = sem("inv_done")
        probs_ready = sem("probs_ready")
        turned = sem("turned")
        pt_hi_done = sem("pt_hi_done")
        pv_done = sem("pv_done")
        out_ready = sem("out_ready")
        stage_read = sem("stage_read")

        def by_group(ap):
            return ap.rearrange("p (w g r) -> p w g r", g=GROUPS, r=H // GROUPS)

        def over_positions(stat):
            return stat.unsqueeze(1).unsqueeze(3).to_broadcast([P, W, GROUPS, H // GROUPS])

        def whole(ap):
            return ap.rearrange("p k n -> p (k n)")

        def grouped_sum_view(ap):
            return whole(ap).rearrange("p (w g r) -> p g w r", g=GROUPS, r=H // GROUPS)

        block = ctx.enter_context(nc.Block())

        @block.sync
        def _(sp):
            sp.dma_start(front[:], x_dram[0]).then_inc(x_in, 16)
            for tile, src in ((wq_sb, w_q), (wk_sb, w_k), (wv_sb, w_v)):
                sp.dma_start(tile[:], src.rearrange("(k p) c -> p k c", p=P)).then_inc(weights_in, 16)
            sp.dma_start(relh_sb[:], rel_h.rearrange("a (k p) b h -> p k (a b h)", p=P)).then_inc(weights_in, 16)
            sp.dma_start(relw_sb[:], rel_w.rearrange("a (k p) w b -> p k (a w b)", p=P)).then_inc(weights_in, 16)
            for tile, src in ((bq_sb, b_q), (bv_sb, b_v)):
                for k in range(KC):
                    sp.dma_start(tile[:, k:k + 1], src.rearrange("(k p a) -> k p a", p=P, a=1)[k]).then_inc(weights_in, 16)
            for h in range(2):
                sp.dma_start(resid[:, h], x_dram[0, :, :, h * HALF:(h + 1) * HALF]).then_inc(resid_in[h], 16)

            def store(b, h):
                sp.wait_ge(out_ready, b * 4 + 2 * h + 2)
                sp.dma_start(out_dram[b, :, :, h * HALF:(h + 1) * HALF], resid[:, h]).then_inc(stored[h], 16)
                sp.wait_ge(stored[h], b * 16 + 16)

            def batch(b, first=False, last=False):
                if not last:
                    sp.wait_ge(z_lo_dve, b + 1)
                    sp.wait_ge(z_lo_pool, b + 1)
                    sp.dma_start(front[:], x_dram[b + 1]).then_inc(x_in, 16)
                if not first:
                    for h in range(2):
                        store(b - 1, h)
                        sp.dma_start(resid[:, h], x_dram[b, :, :, h * HALF:(h + 1) * HALF]).then_inc(resid_in[h], 16)

            batch(0, first=True)
            with sp.Fori(0, B // 2 - 1) as pair:
                batch(pair * 2 + 1)
                batch(pair * 2 + 2)
            batch(B - 1, last=True)
            for h in range(2):
                store(B - 1, h)

        @block.tensor
        def _(pe):
            def prepare():
                pe.wait_ge(weights_in, 16 * WEIGHT_LOADS)
                pe.wait_ge(const_ready, 4)
                for m in range(KC):
                    for k in range(KC):
                        mm = pe.matmul(scores[0][:, m * C:(m + 1) * C], wq_sb[:, k, m * P:(m + 1) * P], wk_sb[:, k, :],
                                       start=(k == 0), stop=(k == KC - 1))
                mm.then_inc(prep_mm, 1)
                for k in range(KC):
                    for c in range(KC):
                        at = HALF + k * C + c * P
                        mm = pe.transpose(scores[0][:, at:at + P], wv_sb[:, c, k * P:(k + 1) * P], ident[:])
                mm.then_inc(prep_mm, 1)
                for m in range(KC):
                    for k in range(KC):
                        mm = pe.matmul(sums[:, 0, m:m + 1], wk_sb[:, k, m * P:(m + 1) * P], bq_sb[:, k:k + 1],
                                       start=(k == 0), stop=(k == KC - 1))
                mm.then_inc(prep_mm, 1)
                pe.wait_ge(rel_ready, KC)
                for m in range(KC):
                    if m == 1:
                        pe.wait_ge(prep_read, 2)
                    for n in range(2):
                        for k in range(KC):
                            mm = pe.matmul(scores[1 - m][:, n * HALF:(n + 1) * HALF], wq_sb[:, k, m * P:(m + 1) * P],
                                           rel_sb[:, k, n * HALF:(n + 1) * HALF], start=(k == 0), stop=(k == KC - 1))
                    mm.then_inc(prep_mm, 1)

            def stage_bank(use):
                if not isinstance(use, int) or use >= 2:
                    pe.wait_ge(stage_read, use - 1)

            def group_stat(nb, which, use, bank):
                pe.wait_ge(sumsq_done if which else sum_done, nb + 1)
                stage_bank(use)
                pe.matmul(stage[bank][:, 0:GROUPS], share[:], part[:, which, :], start=True, stop=True).then_inc(stat_mm, 1)

            def u_chunk(b, z, c, use, bank):
                n, m = c // 2, c % 2
                if c == 0:
                    pe.wait_ge(z_lo_dve, b + 1)
                    pe.wait_ge(z_lo_pool, b + 1)
                stage_bank(use)
                at = slice(n * HALF, (n + 1) * HALF)
                for k in range(KC):
                    w = slice(m * P, (m + 1) * P)
                    pe.matmul(stage[bank][:], at_hi[:, k, w], z_hi[:, z, k, at], start=(k == 0), stop=False)
                    pe.matmul(stage[bank][:], at_hi[:, k, w], z_lo[:, z, k, at], start=False, stop=False)
                    mm = pe.matmul(stage[bank][:], at_lo[:, k, w], z_hi[:, z, k, at], start=False, stop=(k == KC - 1))
                mm.then_inc(u_mm, 1)

            def v_chunk(b, z, c, use, bank):
                stage_bank(use)
                for j in range(2):
                    dst = stage[bank][:, j * C:(j + 1) * C]
                    pos = slice((2 * c + j) * P, (2 * c + j + 1) * P)
                    for k in range(KC):
                        pe.matmul(dst, z_hi[:, z, k, pos], wvt_hi[:, k, :], start=(k == 0), stop=False)
                        pe.matmul(dst, z_hi[:, z, k, pos], wvt_lo[:, k, :], start=False, stop=False)
                        mm = pe.matmul(dst, z_lo[:, z, k, pos], wvt_hi[:, k, :], start=False, stop=(k == KC - 1))
                mm.then_inc(v_mm, 1)

            def score_tile(b, z, s, first):
                if s % TH == 0:
                    pe.wait_ge(u_ready, b * 4 + 2 * (s // TH) + 2)
                if not first or s >= 2:
                    pe.wait_ge(exp_done, b * T + s - 1)
                i = slice(s * P, (s + 1) * P)
                dst = [scores[s % 2][:, n * HALF:(n + 1) * HALF] for n in range(2)]
                for k in range(KC):
                    for w, m in ((u_hi, z_hi), (u_hi, z_lo), (u_lo, z_hi)):
                        for n in range(2):
                            mm = pe.matmul(dst[n], w[:, k, i], m[:, z, k, n * HALF:(n + 1) * HALF],
                                           start=(k == 0 and w is u_hi and m is z_hi), stop=(k == KC - 1 and w is u_lo))
                mm.then_inc(scores_ready, 1)

            def turn_tile(b, s, last, end=False):
                pe.wait_ge(probs_ready, b * T + s)
                for q in range(2):
                    use = stage_use(b, ("turn", s, q), last) - (len(NEXT) if end else 0)
                    stage_bank(use)
                    bank = STAGE.index(("turn", s, q)) % 2 if not last else STAGE_LAST.index(("turn", s, q)) % 2
                    for j in range(4):
                        at = (4 * q + j) * P
                        mm = pe.transpose(stage[bank][:, j * P:(j + 1) * P], probs[:, (s + 1) % 2, at:at + P], ident[:])
                    mm.then_inc(turned, 1)

            def value_product(b, s, last, end=False):
                quarter, h = (s + 3) % 4, 0 if s in (0, 5, 6, 7) else 1
                if s == 5:
                    pe.wait_ge(stage_read, stage_use(b, ("v", 3), last) + 1)
                    if not isinstance(b, int) or b > 0:
                        pe.wait_ge(out_ready, b * 4)
                if s == 1:
                    pe.wait_ge(stage_read, stage_use(b, ("turn", 0, 1), last) + 1 - (len(NEXT) if end else 0))
                    pe.wait_ge(out_ready, b * 4 - 2)
                for j in range(2 * quarter, 2 * quarter + 2):
                    for c in range(KC):
                        w = slice(c * P, (c + 1) * P)
                        pe.matmul(sums[:, c, :], v_hi[:, j, w], pt_hi[:, h, j, :], start=(j == 0), stop=False)
                        pe.matmul(sums[:, c, :], v_hi[:, j, w], pt_lo[:, h, j, :], start=False, stop=False)
                        mm = pe.matmul(sums[:, c, :], v_lo[:, j, w], pt_hi[:, h, j, :], start=False, stop=(j == T - 1))
                mm.then_inc(pv_done, 1)

            def batch(b, z, first=False, last=False):
                for s in range(STEPS):
                    score_tile(b, z, s, first)
                    if not first or s > 0:
                        turn_tile(b, s, last)
                    if not first or s >= 5:
                        value_product(b, s, last)
                    for kind, c in SLOTS[s]:
                        if last and (kind, c) in NEXT:
                            continue
                        use = stage_use(b, (kind, c), last)
                        bank = (STAGE_LAST if last else STAGE).index((kind, c)) % 2
                        if kind == "u":
                            u_chunk(b + (c < 2), (z + (c < 2)) % 2, c, use, bank)
                        elif kind == "v":
                            v_chunk(b, z, c, use, bank)
                        else:
                            group_stat(b + 1, int(kind == "var"), use, bank)

            prepare()
            group_stat(0, 0, 0, 0)
            group_stat(0, 1, 1, 1)
            pe.wait_ge(prep_read, 5)
            u_chunk(0, 0, 0, 2, 0)
            u_chunk(0, 0, 1, 3, 1)
            batch(0, 0, first=True)
            with pe.Fori(0, B // 2 - 1) as pair:
                batch(pair * 2 + 1, 1)
                batch(pair * 2 + 2, 0)
            batch(B - 1, 1, last=True)
            turn_tile(B, 0, False, end=True)
            for s in range(5):
                value_product(B, s, False, end=True)

        @block.scalar
        def _(act):
            def prepare():
                act.preload_act_table(ACT.Exp)
                for n, dst in enumerate((at_hi, wvt_hi)):
                    act.wait_ge(prep_mm, n + 1)
                    act.activation(whole(dst[:]), scores[0][:, n * HALF:(n + 1) * HALF], ACT.Copy).then_inc(prep_hi, 1)

            def square(nb):
                act.wait_ge(centred_dve, nb + 1)
                act.wait_ge(centred_pool, nb + 1)
                act.activation(squares[:], front[:], ACT.Square).then_inc(squared, 1)

            def z_high(nb, z, first):
                for k in range(KC):
                    act.wait_ge(z_scaled, nb * 2 + k + 1)
                    if k == 0 and not first:
                        act.wait_ge(scores_ready, (nb - 1) * T)
                    act.activation(z_hi[:, z, k, :], front[:, k, :], ACT.Copy).then_inc(z_hi_done, 1)

            def u_high(b, c, use, free):
                n, m = c // 2, c % 2
                act.wait_ge(stage_read, use + 1)
                if free is not None:
                    act.wait_ge(scores_ready, free)
                act.activation(u_hi[:, m, n * HALF:(n + 1) * HALF], u_sum[:, c % 2, :], ACT.Copy).then_inc(u_hi_done, 1)

            def v_high(b, c, bank, first):
                act.wait_ge(v_mm, b * 4 + c + 1)
                if not first:
                    act.wait_ge(pv_done, b * 8 - 3 + c)
                act.activation(v_hi[:, 2 * c:2 * c + 2, :].rearrange("p j c -> p (j c)"), stage[bank][:],
                               ACT.Copy).then_inc(v_hi_done, 1)

            def turned_high(b, s, last, first, end=False):
                t = (s - 1) % T
                for q in range(2):
                    bank = STAGE.index(("turn", s, q)) % 2 if not last else STAGE_LAST.index(("turn", s, q)) % 2
                    act.wait_ge(turned, (b * T + s) * 2 - 1 + q)
                    if q == 0 and t % TH == 0 and not first:
                        act.wait_ge(pv_done, b * 8 - 4 + t)
                    at = slice((t % TH) * P, (t % TH + 1) * P)
                    act.activation(pt_hi[:, t // TH, 4 * q:4 * q + 4, at], stage[bank][:].rearrange("p (j i) -> p j i", j=4),
                                   ACT.Copy).then_inc(pt_hi_done, 1)

            def exponent(b, s, first):
                act.wait_ge(max_done, b * T + s + 1)
                if not first or s >= 2:
                    act.wait_ge(turned, (b * T + s) * 2 - 2)
                act.activation(probs[:, s % 2, :], scores[s % 2][:], ACT.Exp, bias=neg_max[:, s % 2:s % 2 + 1],
                               accum_out=row_sum[:, s % 2:s % 2 + 1]).then_inc(exp_done, 1)

            def batch(b, z, first=False, last=False):
                for s in range(STEPS):
                    if not first or s > 0:
                        turned_high(b, s, last, first)
                    exponent(b, s, first)
                    for kind, c in SLOTS[s]:
                        if last and (kind, c) in NEXT:
                            continue
                        use = stage_use(b, (kind, c), last)
                        bank = (STAGE_LAST if last else STAGE).index((kind, c)) % 2
                        if kind == "u":
                            u_high(b, c, use, (b * T + 4 if c < 2 else None if first else b * T))
                        elif kind == "v":
                            v_high(b, c, bank, first)
                    if s == 2 and not last:
                        square(b + 1)
                    if s == 4 and not last:
                        z_high(b + 1, (z + 1) % 2, first)

            prepare()
            square(0)
            z_high(0, 0, True)
            u_high(0, 0, 2, None)
            u_high(0, 1, 3, None)
            batch(0, 0, first=True)
            with act.Fori(0, B // 2 - 1) as pair:
                batch(pair * 2 + 1, 1)
                batch(pair * 2 + 2, 0)
            batch(B - 1, 1, last=True)
            turned_high(B, 0, False, False, end=True)

        @block.vector
        def _(dve):
            def prepare():
                dve.wait_ge(weights_in, 16 * WEIGHT_LOADS)
                for k in range(KC):
                    dve.tensor_tensor(rel_sb[:, k, :].rearrange("p (w h) -> p w h", w=W),
                                      relw_sb[:, k, :].unsqueeze(2).to_broadcast([P, W, H]),
                                      relh_sb[:, k, :].unsqueeze(1).to_broadcast([P, W, H]), ALU.add).then_inc(rel_ready, 1)
                for n, (hi, lo) in enumerate(((at_hi, at_lo), (wvt_hi, wvt_lo))):
                    dve.wait_ge(prep_hi, n + 1)
                    dve.tensor_tensor(whole(lo[:]), scores[0][:, n * HALF:(n + 1) * HALF], whole(hi[:]).bitcast(F32),
                                      ALU.subtract).then_inc(prep_read, 1)
                dve.wait_ge(prep_mm, 3)
                dve.tensor_copy(kb_sb[:], sums[:, 0, 0:KC]).then_inc(prep_read, 1)
                dve.wait_ge(prep_read, 3)
                for m in range(KC):
                    dve.wait_ge(prep_mm, 4 + m)
                    dve.tensor_scalar(r_bias[:, m, :], scores[1 - m][:], kb_sb[:, m:m + 1], None, ALU.add).then_inc(prep_read, 1)

            def sum_x(nb):
                dve.wait_ge(x_in, nb * 16 + 16)
                dve.tensor_reduce(part[:, 0, :], grouped_sum_view(front[:]), AX.XY, ALU.add).then_inc(sum_done, 1)

            def sum_squares(nb):
                dve.wait_ge(squared, nb + 1)
                dve.tensor_reduce(part[:, 1, :], grouped_sum_view(squares[:]), AX.XY, ALU.add).then_inc(sumsq_done, 1)

            def read_mean(nb, bank):
                dve.wait_ge(stat_mm, nb * 2 + 1)
                dve.tensor_copy(mean[:], stage[bank][:, 0:GROUPS]).then_inc(stage_read, 1)

            def centre(nb, use):
                dve.wait_ge(stage_read, use + 1)
                f = by_group(front[:, 0, :])
                dve.tensor_tensor(f, f, over_positions(mean[:]), ALU.subtract).then_inc(centred_dve, 1)

            def read_var(nb, bank):
                dve.wait_ge(stat_mm, nb * 2 + 2)
                dve.tensor_scalar(var_eps[:], stage[bank][:, 0:GROUPS], EPS, None, ALU.add).then_inc(stage_read, 1)

            def z_low(nb, z):
                dve.wait_ge(z_hi_done, nb * 2 + 1)
                dve.tensor_tensor(z_lo[:, z, 0, :], front[:, 0, :], z_hi[:, z, 0, :].bitcast(F32),
                                  ALU.subtract).then_inc(z_lo_dve, 1)

            def u_add(b, c, bank, first):
                n, m = c // 2, c % 2
                dve.wait_ge(u_mm, b * 4 + c + 1)
                if not first:
                    dve.wait_ge(u_ready, b * 4 + c - 1)
                dve.tensor_tensor(u_sum[:, c % 2, :], stage[bank][:], r_bias[:, m, n * HALF:(n + 1) * HALF],
                                  ALU.add).then_inc(stage_read, 1)

            def v_low(b, c, bank):
                dve.wait_ge(v_hi_done, b * 4 + c + 1)
                at = slice(2 * c, 2 * c + 2)
                dve.tensor_tensor(v_lo[:, at, :].rearrange("p j c -> p (j c)"), stage[bank][:],
                                  v_hi[:, at, :].rearrange("p j c -> p (j c)").bitcast(F32), ALU.subtract).then_inc(stage_read, 1)

            def turned_low(b, s, last):
                t = (s - 1) % T
                for q in range(2):
                    bank = STAGE.index(("turn", s, q)) % 2 if not last else STAGE_LAST.index(("turn", s, q)) % 2
                    at = slice((t % TH) * P, (t % TH + 1) * P)
                    dve.wait_ge(pt_hi_done, (b * T + s) * 2 - 1 + q)
                    dve.tensor_tensor(pt_lo[:, t // TH, 4 * q:4 * q + 4, at], stage[bank][:].rearrange("p (j i) -> p j i", j=4),
                                      pt_hi[:, t // TH, 4 * q:4 * q + 4, at].bitcast(F32), ALU.subtract).then_inc(stage_read, 1)

            def row_max(b, s):
                dve.wait_ge(scores_ready, b * T + s + 1)
                dve.tensor_reduce(neg_max[:, s % 2:s % 2 + 1], scores[s % 2][:], AX.X, ALU.max, negate=True).then_inc(max_done, 1)

            def normalise(b, s):
                at = slice(s % 2, s % 2 + 1)
                dve.wait_ge(exp_done, b * T + s + 1)
                dve.reciprocal(row_inv[:, at], row_sum[:, at]).then_inc(inv_done, 1)
                dve.wait_ge(inv_done, b * T + s + 1)
                dve.tensor_scalar(probs[:, s % 2, :], probs[:, s % 2, :], row_inv[:, at], None, ALU.mult).then_inc(probs_ready, 1)

            def finish(b, h):
                dve.wait_ge(pv_done, b * 8 + 4 * h + 4)
                dve.wait_ge(resid_in[h], b * 16 + 16)
                for c in range(KC):
                    dve.scalar_tensor_tensor(out=resid[:, h, c, :], in0=sums[:, c, :], scalar=bv_sb[:, c:c + 1],
                                             in1=resid[:, h, c, :], op0=ALU.add, op1=ALU.add).then_inc(out_ready, 1)

            def batch(b, z, first=False, last=False):
                for s in range(STEPS):
                    row_max(b, s)
                    if not first or s > 0:
                        turned_low(b, s, last)
                    normalise(b, s)
                    if not first and s in (0, 4):
                        finish(b - 1, s // 4)
                    for kind, c in SLOTS[s]:
                        if last and (kind, c) in NEXT:
                            continue
                        bank = (STAGE_LAST if last else STAGE).index((kind, c)) % 2
                        if kind == "u":
                            u_add(b + (c < 2), c, bank, False)
                        elif kind == "v":
                            v_low(b, c, bank)
                        elif kind == "mean":
                            read_mean(b + 1, bank)
                        else:
                            read_var(b + 1, bank)
                    if not last:
                        if s == 0:
                            sum_x(b + 1)
                        if s == 1:
                            centre(b + 1, stage_use(b, ("mean", 0)))
                        if s == 2:
                            sum_squares(b + 1)
                        if s == 4:
                            z_low(b + 1, (z + 1) % 2)

            sum_x(0)
            prepare()
            read_mean(0, 0)
            centre(0, 0)
            sum_squares(0)
            read_var(0, 1)
            z_low(0, 0)
            u_add(0, 0, 0, True)
            u_add(0, 1, 1, True)
            batch(0, 0, first=True)
            with dve.Fori(0, B // 2 - 1) as pair:
                batch(pair * 2 + 1, 1)
                batch(pair * 2 + 2, 0)
            batch(B - 1, 1, last=True)
            turned_low(B, 0, False)
            finish(B - 1, 0)
            finish(B - 1, 1)

        @block.gpsimd
        def _(pool):
            def prepare():
                pool.memset(ident[:], 0.0).then_inc(const_ready, 1)
                pool.memset(share[:], 1.0 / COUNT).then_inc(const_ready, 1)
                pool.memset(power[:], -0.5).then_inc(const_ready, 1)
                pool.wait_ge(const_ready, 3)
                pool.affine_select(out=ident[:], in_=ident[:], compare_op=ALU.not_equal, fill=1.0, base=0,
                                   pattern=[[-1, P]], channel_multiplier=1).then_inc(const_ready, 1)

            def centre(nb, use):
                pool.wait_ge(stage_read, use + 1)
                f = by_group(front[:, 1, :])
                pool.tensor_tensor(f, f, over_positions(mean[:]), ALU.subtract).then_inc(centred_pool, 1)

            def scale_z(nb, z, use):
                pool.wait_ge(stage_read, use + 1)
                pool.tensor_tensor(rstd[:], var_eps[:], power[:], ALU.pow).then_inc(rstd_done, 1)
                pool.wait_ge(rstd_done, nb + 1)
                for k in range(KC):
                    f = by_group(front[:, k, :])
                    pool.tensor_tensor(f, f, over_positions(rstd[:]), ALU.mult).then_inc(z_scaled, 1)
                pool.wait_ge(z_hi_done, nb * 2 + 2)
                pool.tensor_tensor(z_lo[:, z, 1, :], front[:, 1, :], z_hi[:, z, 1, :].bitcast(F32),
                                   ALU.subtract).then_inc(z_lo_pool, 1)

            def u_low(b, c):
                n, m = c // 2, c % 2
                at = slice(n * HALF, (n + 1) * HALF)
                pool.wait_ge(u_hi_done, b * 4 + c + 1)
                pool.tensor_tensor(u_lo[:, m, at], u_sum[:, c % 2, :], u_hi[:, m, at].bitcast(F32),
                                   ALU.subtract).then_inc(u_ready, 1)

            def batch(b, z, last=False):
                u_low(b, 2)
                u_low(b, 3)
                if not last:
                    centre(b + 1, stage_use(b, ("mean", 0)))
                    scale_z(b + 1, (z + 1) % 2, stage_use(b, ("var", 0)))
                    u_low(b + 1, 0)
                    u_low(b + 1, 1)

            prepare()
            centre(0, 0)
            scale_z(0, 0, 1)
            u_low(0, 0)
            u_low(0, 1)
            batch(0, 0)
            with pool.Fori(0, B // 2 - 1) as pair:
                batch(pair * 2 + 1, 1)
                batch(pair * 2 + 2, 0)
            batch(B - 1, 1, last=True)


def kernel(**inputs):
    import numpy as np
    import concourse.bacc as bacc
    from concourse.bass_utils import run_bass_kernel_spmd

    names = ["x", "L0_conv_Wq", "L0_conv_bq", "L0_conv_Wk", "L0_conv_Wv", "L0_conv_bv", "L0_conv_rel_h", "L0_conv_rel_w"]
    nc = bacc.Bacc("TRN2", target_bir_lowering=False, num_devices=1)
    arrays, args = {}, []
    for name in names:
        a = np.ascontiguousarray(inputs[name])
        arrays[f"in_{name}"] = a
        args.append(nc.dram_tensor(f"in_{name}", a.shape, mybir.dt.from_np(a.dtype), kind="ExternalInput").ap())
    x = inputs["x"]
    args.append(nc.dram_tensor("out", x.shape, mybir.dt.from_np(np.dtype(x.dtype)), kind="ExternalOutput").ap())
    attention_block(nc, *args)
    result = run_bass_kernel_spmd(nc, [arrays], core_ids=[0])
    return result.results[0]["out"]
```

```python
from contextlib import ExitStack

import concourse.bass as bass
from concourse import mybir

F32 = mybir.dt.float32
F32R = mybir.dt.float32r
ALU = mybir.AluOpType
ACT = mybir.ActivationFunctionType
AX = mybir.AxisListType

P = 128
GROUPS = 16
EPS = 1e-5
STEPS = 8
SLOTS = {0: [("u", 2)], 1: [("u", 3), ("v", 0), ("mean", 0)], 2: [("v", 1)], 3: [("v", 2), ("var", 0)],
         4: [("v", 3)], 5: [("u", 0)], 6: [("u", 1)], 7: []}
NEXT = [("mean", 0), ("var", 0), ("u", 0), ("u", 1)]
STAGE = [use for s in range(STEPS) for use in [("turn", s, 0), ("turn", s, 1), *SLOTS[s]]]
STAGE_LAST = [use for use in STAGE if use not in NEXT]
PER_BATCH = len(STAGE)


def stage_use(b, use, last=False):
    order = STAGE_LAST if last else STAGE
    return b * PER_BATCH + len(NEXT) - 2 + order.index(use)


def attention_block(nc, x, w_q, b_q, w_k, w_v, b_v, rel_h, rel_w, out):
    B, C, W, H = x.shape
    N = W * H
    KC = C // P
    T = N // P
    HALF = N // 2
    TH = T // 2
    Q = P * 4
    WEIGHT_LOADS = 5 + 2 * KC
    PREP_READS = 2 + 3 + KC
    COUNT = C * W * H // GROUPS
    assert KC == 2 and T == STEPS and HALF == Q and B % 2 == 0 and PER_BATCH % 2 == 0

    x_dram = x.rearrange("b (k p) w h -> b p k (w h)", p=P)
    out_dram = out.rearrange("b (k p) w h -> b p k (w h)", p=P)

    with ExitStack() as ctx:
        def sb(name, shape, dt=F32):
            return ctx.enter_context(nc.sbuf_tensor(name, shape, dt))

        def sem(name):
            return ctx.enter_context(nc.semaphore(name))

        z_hi = sb("z_hi", [P, 2, KC, N], F32R)
        z_lo = sb("z_lo", [P, 2, KC, N], F32R)
        u_hi = sb("u_hi", [P, KC, N], F32R)
        u_lo = sb("u_lo", [P, KC, N], F32R)
        v_hi = sb("v_hi", [P, T, C], F32R)
        v_lo = sb("v_lo", [P, T, C], F32R)
        pt_hi = sb("pt_hi", [P, 2, T, HALF], F32R)
        pt_lo = sb("pt_lo", [P, 2, T, HALF], F32R)
        at_hi = sb("at_hi", [P, KC, C], F32R)
        at_lo = sb("at_lo", [P, KC, C], F32R)
        wvt_hi = sb("wvt_hi", [P, KC, C], F32R)
        wvt_lo = sb("wvt_lo", [P, KC, C], F32R)
        front = sb("front", [P, KC, N])
        squares = sb("squares", [P, KC, N])
        resid = sb("resid", [P, 2, KC, HALF])
        probs = sb("probs", [P, 2, N])
        u_sum = sb("u_sum", [P, 2, HALF])
        r_bias = sb("r_bias", [P, KC, N])
        wq_sb = sb("wq_sb", [P, KC, C])
        wk_sb = sb("wk_sb", [P, KC, C])
        wv_sb = sb("wv_sb", [P, KC, C])
        bq_sb = sb("bq_sb", [P, KC])
        bv_sb = sb("bv_sb", [P, KC])
        rel_sb = sb("rel_sb", [P, KC, H + W])
        relq_sb = sb("relq_sb", [P, KC, H + W])
        relh_kb = sb("relh_kb", [P, KC, H])
        kb_sb = sb("kb_sb", [P, KC])
        ident = sb("ident", [P, P])
        share = sb("share", [P, P])
        power = sb("power", [P, GROUPS])
        part = sb("part", [P, 2, GROUPS])
        mean = sb("mean", [P, GROUPS])
        var_eps = sb("var_eps", [P, GROUPS])
        rstd = sb("rstd", [P, GROUPS])
        neg_max = sb("neg_max", [P, 2])
        row_sum = sb("row_sum", [P, 2])
        row_inv = sb("row_inv", [P, 2])

        scores = [ctx.enter_context(nc.psum_tensor(f"scores{i}", [P, N], F32)) for i in range(2)]
        sums = ctx.enter_context(nc.psum_tensor("sums", [P, KC, HALF], F32))
        stage = [ctx.enter_context(nc.psum_tensor(f"stage{i}", [P, Q], F32)) for i in range(2)]

        weights_in = sem("weights_in")
        x_in = sem("x_in")
        resid_in = [sem(f"resid_in{h}") for h in range(2)]
        stored = [sem(f"stored{h}") for h in range(2)]
        const_ready = sem("const_ready")
        prep_mm = sem("prep_mm")
        prep_hi = sem("prep_hi")
        prep_read = sem("prep_read")
        sum_done = sem("sum_done")
        sumsq_done = sem("sumsq_done")
        stat_mm = sem("stat_mm")
        centred = sem("centred")
        squared = sem("squared")
        rstd_done = sem("rstd_done")
        z_scaled = sem("z_scaled")
        z_hi_done = sem("z_hi_done")
        z_lo_done0 = sem("z_lo_done0")
        z_lo_done1 = sem("z_lo_done1")
        u_mm = sem("u_mm")
        u_hi_done = sem("u_hi_done")
        u_ready = sem("u_ready")
        v_mm = sem("v_mm")
        v_hi_done = sem("v_hi_done")
        scores_ready = sem("scores_ready")
        max_done = sem("max_done")
        exp_done = sem("exp_done")
        inv_done = sem("inv_done")
        probs_ready = sem("probs_ready")
        turned = sem("turned")
        pt_hi_done = sem("pt_hi_done")
        pv_done = sem("pv_done")
        out_ready = sem("out_ready")
        stage_read = sem("stage_read")

        def by_group(ap):
            return ap.rearrange("p (w g r) -> p w g r", g=GROUPS, r=H // GROUPS)

        def over_positions(stat):
            return stat.unsqueeze(1).unsqueeze(3).to_broadcast([P, W, GROUPS, H // GROUPS])

        def whole(ap):
            return ap.rearrange("p k n -> p (k n)")

        def grouped_sum_view(ap):
            return whole(ap).rearrange("p (w g r) -> p g w r", g=GROUPS, r=H // GROUPS)

        block = ctx.enter_context(nc.Block())

        @block.sync
        def _(sp):
            sp.dma_start(front[:], x_dram[0]).then_inc(x_in, 16)
            for h in range(2):
                sp.dma_start(resid[:, h], x_dram[0, :, :, h * HALF:(h + 1) * HALF]).then_inc(resid_in[h], 16)

            def store(b, h):
                sp.wait_ge(out_ready, b * 4 + 2 * h + 2)
                sp.dma_start(out_dram[b, :, :, h * HALF:(h + 1) * HALF], resid[:, h]).then_inc(stored[h], 16)
                sp.wait_ge(stored[h], b * 16 + 16)

            def batch(b, first=False, last=False):
                if not last:
                    sp.wait_ge(z_lo_done0, b + 1)
                    sp.wait_ge(z_lo_done1, b + 1)
                    sp.dma_start(front[:], x_dram[b + 1]).then_inc(x_in, 16)
                if not first:
                    for h in range(2):
                        store(b - 1, h)
                        sp.dma_start(resid[:, h], x_dram[b, :, :, h * HALF:(h + 1) * HALF]).then_inc(resid_in[h], 16)

            batch(0, first=True)
            with sp.Fori(0, B // 2 - 1) as pair:
                batch(pair * 2 + 1)
                batch(pair * 2 + 2)
            batch(B - 1, last=True)
            for h in range(2):
                store(B - 1, h)

        @block.tensor
        def _(pe):
            def prepare_a():
                pe.wait_ge(weights_in, 16 * WEIGHT_LOADS)
                for m in range(KC):
                    for k in range(KC):
                        mm = pe.matmul(scores[0][:, m * C:(m + 1) * C], wq_sb[:, k, m * P:(m + 1) * P], wk_sb[:, k, :],
                                       start=(k == 0), stop=(k == KC - 1))
                mm.then_inc(prep_mm, 1)

            def prepare_rest():
                for k in range(KC):
                    for c in range(KC):
                        at = HALF + k * C + c * P
                        mm = pe.transpose(scores[0][:, at:at + P], wv_sb[:, c, k * P:(k + 1) * P], ident[:])
                mm.then_inc(prep_mm, 1)
                for m in range(KC):
                    for k in range(KC):
                        pe.matmul(sums[:, 0, m:m + 1], wk_sb[:, k, m * P:(m + 1) * P], bq_sb[:, k:k + 1],
                                  start=(k == 0), stop=(k == KC - 1))
                for m in range(KC):
                    at = m * (H + W)
                    for k in range(KC):
                        mm = pe.matmul(sums[:, 1, at:at + H + W], wq_sb[:, k, m * P:(m + 1) * P], rel_sb[:, k, :],
                                       start=(k == 0), stop=(k == KC - 1))
                mm.then_inc(prep_mm, 1)

            def stage_bank(use):
                if not isinstance(use, int) or use >= 2:
                    pe.wait_ge(stage_read, use - 1)

            def group_stat(nb, which, use, bank):
                pe.wait_ge(sumsq_done if which else sum_done, nb + 1)
                stage_bank(use)
                pe.matmul(stage[bank][:, 0:GROUPS], share[:], part[:, which, :], start=True, stop=True).then_inc(stat_mm, 1)

            def u_chunk(b, z, c, use, bank):
                n, m = c // 2, c % 2
                if c == 0:
                    pe.wait_ge(z_lo_done0, b + 1)
                    pe.wait_ge(z_lo_done1, b + 1)
                stage_bank(use)
                at = slice(n * HALF, (n + 1) * HALF)
                for k in range(KC):
                    w = slice(m * P, (m + 1) * P)
                    pe.matmul(stage[bank][:], at_hi[:, k, w], z_hi[:, z, k, at], start=(k == 0), stop=False)
                    pe.matmul(stage[bank][:], at_hi[:, k, w], z_lo[:, z, k, at], start=False, stop=False)
                    mm = pe.matmul(stage[bank][:], at_lo[:, k, w], z_hi[:, z, k, at], start=False, stop=(k == KC - 1))
                mm.then_inc(u_mm, 1)

            def v_chunk(b, z, c, use, bank):
                stage_bank(use)
                for j in range(2):
                    dst = stage[bank][:, j * C:(j + 1) * C]
                    pos = slice((2 * c + j) * P, (2 * c + j + 1) * P)
                    for k in range(KC):
                        pe.matmul(dst, z_hi[:, z, k, pos], wvt_hi[:, k, :], start=(k == 0), stop=False)
                        pe.matmul(dst, z_hi[:, z, k, pos], wvt_lo[:, k, :], start=False, stop=False)
                        mm = pe.matmul(dst, z_lo[:, z, k, pos], wvt_hi[:, k, :], start=False, stop=(k == KC - 1))
                mm.then_inc(v_mm, 1)

            def score_tile(b, z, s, first):
                if s % TH == 0:
                    pe.wait_ge(u_ready, b * 4 + 2 * (s // TH) + 2)
                if not first or s >= 2:
                    pe.wait_ge(exp_done, b * T + s - 1)
                i = slice(s * P, (s + 1) * P)
                dst = [scores[s % 2][:, n * HALF:(n + 1) * HALF] for n in range(2)]
                for k in range(KC):
                    for w, m in ((u_hi, z_hi), (u_hi, z_lo), (u_lo, z_hi)):
                        for n in range(2):
                            mm = pe.matmul(dst[n], w[:, k, i], m[:, z, k, n * HALF:(n + 1) * HALF],
                                           start=(k == 0 and w is u_hi and m is z_hi), stop=(k == KC - 1 and w is u_lo))
                mm.then_inc(scores_ready, 1)

            def turn_tile(b, s, last, end=False):
                pe.wait_ge(probs_ready, b * T + s)
                for q in range(2):
                    use = stage_use(b, ("turn", s, q), last) - (len(NEXT) if end else 0)
                    stage_bank(use)
                    bank = STAGE.index(("turn", s, q)) % 2 if not last else STAGE_LAST.index(("turn", s, q)) % 2
                    for j in range(4):
                        at = (4 * q + j) * P
                        mm = pe.transpose(stage[bank][:, j * P:(j + 1) * P], probs[:, (s + 1) % 2, at:at + P], ident[:])
                    mm.then_inc(turned, 1)

            def value_product(b, s, last, end=False):
                quarter, h = (s + 3) % 4, 0 if s in (0, 5, 6, 7) else 1
                if s == 5:
                    pe.wait_ge(stage_read, stage_use(b, ("v", 3), last) + 1)
                    if not isinstance(b, int) or b > 0:
                        pe.wait_ge(out_ready, b * 4)
                if s == 1:
                    pe.wait_ge(stage_read, stage_use(b, ("turn", 0, 1), last) + 1 - (len(NEXT) if end else 0))
                    pe.wait_ge(out_ready, b * 4 - 2)
                for j in range(2 * quarter, 2 * quarter + 2):
                    for c in range(KC):
                        w = slice(c * P, (c + 1) * P)
                        pe.matmul(sums[:, c, :], v_hi[:, j, w], pt_hi[:, h, j, :], start=(j == 0), stop=False)
                        pe.matmul(sums[:, c, :], v_hi[:, j, w], pt_lo[:, h, j, :], start=False, stop=False)
                        mm = pe.matmul(sums[:, c, :], v_lo[:, j, w], pt_hi[:, h, j, :], start=False, stop=(j == T - 1))
                mm.then_inc(pv_done, 1)

            def batch(b, z, first=False, last=False):
                for s in range(STEPS):
                    score_tile(b, z, s, first)
                    if not first or s > 0:
                        turn_tile(b, s, last)
                    if not first or s >= 5:
                        value_product(b, s, last)
                    for kind, c in SLOTS[s]:
                        if last and (kind, c) in NEXT:
                            continue
                        use = stage_use(b, (kind, c), last)
                        bank = (STAGE_LAST if last else STAGE).index((kind, c)) % 2
                        if kind == "u":
                            u_chunk(b + (c < 2), (z + (c < 2)) % 2, c, use, bank)
                        elif kind == "v":
                            v_chunk(b, z, c, use, bank)
                        else:
                            group_stat(b + 1, int(kind == "var"), use, bank)

            pe.wait_ge(const_ready, 4)
            group_stat(0, 0, 0, 0)
            prepare_a()
            group_stat(0, 1, 1, 1)
            prepare_rest()
            pe.wait_ge(prep_read, PREP_READS)
            u_chunk(0, 0, 0, 2, 0)
            u_chunk(0, 0, 1, 3, 1)
            batch(0, 0, first=True)
            with pe.Fori(0, B // 2 - 1) as pair:
                batch(pair * 2 + 1, 1)
                batch(pair * 2 + 2, 0)
            batch(B - 1, 1, last=True)
            turn_tile(B, 0, False, end=True)
            for s in range(5):
                value_product(B, s, False, end=True)

        @block.scalar
        def _(act):
            def prepare():
                for tile, src in ((wq_sb, w_q), (wk_sb, w_k), (wv_sb, w_v)):
                    act.dma_start(tile[:], src.rearrange("(k p) c -> p k c", p=P)).then_inc(weights_in, 16)
                for tile, src in ((bq_sb, b_q), (bv_sb, b_v)):
                    for k in range(KC):
                        act.dma_start(tile[:, k:k + 1], src.rearrange("(k p a) -> k p a", p=P, a=1)[k]).then_inc(weights_in, 16)
                act.dma_start(rel_sb[:, :, 0:H], rel_h.rearrange("a (k p) b h -> p k (a b h)", p=P)).then_inc(weights_in, 16)
                act.dma_start(rel_sb[:, :, H:], rel_w.rearrange("a (k p) w b -> p k (a w b)", p=P)).then_inc(weights_in, 16)
                act.preload_act_table(ACT.Exp)

            def prepare_high():
                for n, dst in enumerate((at_hi, wvt_hi)):
                    act.wait_ge(prep_mm, n + 1)
                    act.activation(whole(dst[:]), scores[0][:, n * HALF:(n + 1) * HALF], ACT.Copy).then_inc(prep_hi, 1)

            def square(nb, prologue=False):
                for k in range(KC):
                    act.wait_ge(centred, k + 1 if prologue else nb * KC + KC)
                    act.activation(squares[:, k], front[:, k], ACT.Square).then_inc(squared, 1)

            def z_high(nb, z, first, prologue=False):
                for k in range(KC):
                    act.wait_ge(z_scaled, KC if prologue else nb * 2 + k + 1)
                    if k == 0 and not first:
                        act.wait_ge(scores_ready, (nb - 1) * T)
                    act.activation(z_hi[:, z, k, :], front[:, k, :], ACT.Copy).then_inc(z_hi_done, 1)

            def u_high(b, c, use, free):
                n, m = c // 2, c % 2
                act.wait_ge(stage_read, use + 1)
                if free is not None:
                    act.wait_ge(scores_ready, free)
                act.activation(u_hi[:, m, n * HALF:(n + 1) * HALF], u_sum[:, c % 2, :], ACT.Copy).then_inc(u_hi_done, 1)

            def v_high(b, c, bank, first):
                act.wait_ge(v_mm, b * 4 + c + 1)
                if not first:
                    act.wait_ge(pv_done, b * 8 - 3 + c)
                act.activation(v_hi[:, 2 * c:2 * c + 2, :].rearrange("p j c -> p (j c)"), stage[bank][:],
                               ACT.Copy).then_inc(v_hi_done, 1)

            def turned_high(b, s, last, first, end=False):
                t = (s - 1) % T
                for q in range(2):
                    bank = STAGE.index(("turn", s, q)) % 2 if not last else STAGE_LAST.index(("turn", s, q)) % 2
                    act.wait_ge(turned, (b * T + s) * 2 - 1 + q)
                    if q == 0 and t % TH == 0 and not first:
                        act.wait_ge(pv_done, b * 8 - 4 + t)
                    at = slice((t % TH) * P, (t % TH + 1) * P)
                    act.activation(pt_hi[:, t // TH, 4 * q:4 * q + 4, at], stage[bank][:].rearrange("p (j i) -> p j i", j=4),
                                   ACT.Copy).then_inc(pt_hi_done, 1)

            def exponent(b, s, first):
                act.wait_ge(max_done, b * T + s + 1)
                if not first or s >= 2:
                    act.wait_ge(turned, (b * T + s) * 2 - 2)
                act.activation(probs[:, s % 2, :], scores[s % 2][:], ACT.Exp, bias=neg_max[:, s % 2:s % 2 + 1],
                               accum_out=row_sum[:, s % 2:s % 2 + 1]).then_inc(exp_done, 1)

            def batch(b, z, first=False, last=False):
                for s in range(STEPS):
                    if not first or s > 0:
                        turned_high(b, s, last, first)
                    exponent(b, s, first)
                    if s == 2 and not last:
                        square(b + 1)
                    for kind, c in SLOTS[s]:
                        if last and (kind, c) in NEXT:
                            continue
                        use = stage_use(b, (kind, c), last)
                        bank = (STAGE_LAST if last else STAGE).index((kind, c)) % 2
                        if kind == "u":
                            u_high(b, c, use, (b * T + 4 if c < 2 else None if first else b * T))
                        elif kind == "v":
                            v_high(b, c, bank, first)
                    if s == 4 and not last:
                        z_high(b + 1, (z + 1) % 2, first)

            prepare()
            square(0, prologue=True)
            prepare_high()
            z_high(0, 0, True, prologue=True)
            u_high(0, 0, 2, None)
            u_high(0, 1, 3, None)
            batch(0, 0, first=True)
            with act.Fori(0, B // 2 - 1) as pair:
                batch(pair * 2 + 1, 1)
                batch(pair * 2 + 2, 0)
            batch(B - 1, 1, last=True)
            turned_high(B, 0, False, False, end=True)

        @block.vector
        def _(dve):
            def prepare_low():
                for n, (hi, lo) in enumerate(((at_hi, at_lo), (wvt_hi, wvt_lo))):
                    dve.wait_ge(prep_hi, n + 1)
                    dve.tensor_tensor(whole(lo[:]), scores[0][:, n * HALF:(n + 1) * HALF], whole(hi[:]).bitcast(F32),
                                      ALU.subtract).then_inc(prep_read, 1)

            def prepare_bias():
                dve.wait_ge(prep_mm, 3)
                dve.tensor_copy(kb_sb[:], sums[:, 0, 0:KC]).then_inc(prep_read, 1)
                dve.tensor_copy(whole(relq_sb[:]), sums[:, 1, 0:KC * (H + W)]).then_inc(prep_read, 1)
                dve.wait_ge(prep_read, 4)
                dve.tensor_tensor(relh_kb[:], relq_sb[:, :, 0:H], kb_sb[:].unsqueeze(2).to_broadcast([P, KC, H]),
                                  ALU.add).then_inc(prep_read, 1)
                dve.wait_ge(prep_read, 5)
                for m in range(KC):
                    dve.tensor_tensor(r_bias[:, m, :].rearrange("p (w h) -> p w h", w=W),
                                      relq_sb[:, m, H:].unsqueeze(2).to_broadcast([P, W, H]),
                                      relh_kb[:, m, :].unsqueeze(1).to_broadcast([P, W, H]), ALU.add).then_inc(prep_read, 1)

            def sum_x(nb):
                dve.wait_ge(x_in, nb * 16 + 16)
                dve.tensor_reduce(part[:, 0, :], grouped_sum_view(front[:]), AX.XY, ALU.add).then_inc(sum_done, 1)

            def sum_squares(nb):
                dve.wait_ge(squared, nb * KC + KC)
                dve.tensor_reduce(part[:, 1, :], grouped_sum_view(squares[:]), AX.XY, ALU.add).then_inc(sumsq_done, 1)

            def read_mean(nb, bank):
                dve.wait_ge(stat_mm, nb * 2 + 1)
                dve.tensor_copy(mean[:], stage[bank][:, 0:GROUPS]).then_inc(stage_read, 1)

            def centre(nb, k, use):
                dve.wait_ge(stage_read, use + 1)
                f = by_group(front[:, k, :])
                dve.tensor_tensor(f, f, over_positions(mean[:]), ALU.subtract).then_inc(centred, 1)

            def read_var(nb, bank):
                dve.wait_ge(stat_mm, nb * 2 + 2)
                dve.tensor_scalar(var_eps[:], stage[bank][:, 0:GROUPS], EPS, None, ALU.add).then_inc(stage_read, 1)

            def z_low(nb, z, k, done):
                dve.wait_ge(z_hi_done, nb * KC + k + 1)
                dve.tensor_tensor(z_lo[:, z, k, :], front[:, k, :], z_hi[:, z, k, :].bitcast(F32),
                                  ALU.subtract).then_inc(done, 1)

            def u_add(b, c, bank, first):
                n, m = c // 2, c % 2
                dve.wait_ge(u_mm, b * 4 + c + 1)
                if not first:
                    dve.wait_ge(u_ready, b * 4 + c - 1)
                dve.tensor_tensor(u_sum[:, c % 2, :], stage[bank][:], r_bias[:, m, n * HALF:(n + 1) * HALF],
                                  ALU.add).then_inc(stage_read, 1)

            def v_low(b, c, bank):
                dve.wait_ge(v_hi_done, b * 4 + c + 1)
                at = slice(2 * c, 2 * c + 2)
                dve.tensor_tensor(v_lo[:, at, :].rearrange("p j c -> p (j c)"), stage[bank][:],
                                  v_hi[:, at, :].rearrange("p j c -> p (j c)").bitcast(F32), ALU.subtract).then_inc(stage_read, 1)

            def turned_low(b, s, last):
                t = (s - 1) % T
                for q in range(2):
                    bank = STAGE.index(("turn", s, q)) % 2 if not last else STAGE_LAST.index(("turn", s, q)) % 2
                    at = slice((t % TH) * P, (t % TH + 1) * P)
                    dve.wait_ge(pt_hi_done, (b * T + s) * 2 - 1 + q)
                    dve.tensor_tensor(pt_lo[:, t // TH, 4 * q:4 * q + 4, at], stage[bank][:].rearrange("p (j i) -> p j i", j=4),
                                      pt_hi[:, t // TH, 4 * q:4 * q + 4, at].bitcast(F32), ALU.subtract).then_inc(stage_read, 1)

            def row_max(b, s):
                dve.wait_ge(scores_ready, b * T + s + 1)
                dve.tensor_reduce(neg_max[:, s % 2:s % 2 + 1], scores[s % 2][:], AX.X, ALU.max, negate=True).then_inc(max_done, 1)

            def normalise(b, s):
                at = slice(s % 2, s % 2 + 1)
                dve.wait_ge(exp_done, b * T + s + 1)
                dve.reciprocal(row_inv[:, at], row_sum[:, at]).then_inc(inv_done, 1)
                dve.wait_ge(inv_done, b * T + s + 1)
                dve.tensor_scalar(probs[:, s % 2, :], probs[:, s % 2, :], row_inv[:, at], None, ALU.mult).then_inc(probs_ready, 1)

            def finish(b, h):
                dve.wait_ge(pv_done, b * 8 + 4 * h + 4)
                dve.wait_ge(resid_in[h], b * 16 + 16)
                for c in range(KC):
                    dve.scalar_tensor_tensor(out=resid[:, h, c, :], in0=sums[:, c, :], scalar=bv_sb[:, c:c + 1],
                                             in1=resid[:, h, c, :], op0=ALU.add, op1=ALU.add).then_inc(out_ready, 1)

            def batch(b, z, first=False, last=False):
                for s in range(STEPS):
                    row_max(b, s)
                    if not first or s > 0:
                        turned_low(b, s, last)
                    normalise(b, s)
                    if not first and s in (0, 4):
                        finish(b - 1, s // 4)
                    for kind, c in SLOTS[s]:
                        if last and (kind, c) in NEXT:
                            continue
                        bank = (STAGE_LAST if last else STAGE).index((kind, c)) % 2
                        if kind == "u":
                            u_add(b + (c < 2), c, bank, False)
                        elif kind == "v":
                            v_low(b, c, bank)
                        elif kind == "mean":
                            read_mean(b + 1, bank)
                        else:
                            read_var(b + 1, bank)
                    if not last:
                        if s == 0:
                            sum_x(b + 1)
                        if s == 1:
                            centre(b + 1, 0, stage_use(b, ("mean", 0)))
                        if s == 2:
                            sum_squares(b + 1)
                        if s == 4:
                            z_low(b + 1, (z + 1) % 2, 0, z_lo_done0)

            sum_x(0)
            read_mean(0, 0)
            centre(0, 0, 0)
            centre(0, 1, 0)
            sum_squares(0)
            read_var(0, 1)
            prepare_low()
            dve.wait_ge(rstd_done, 1)
            f0 = by_group(front[:, 0, :])
            dve.tensor_tensor(f0, f0, over_positions(rstd[:]), ALU.mult).then_inc(z_scaled, 1)
            prepare_bias()
            z_low(0, 0, 0, z_lo_done0)
            z_low(0, 0, 1, z_lo_done1)
            u_add(0, 0, 0, True)
            u_add(0, 1, 1, True)
            batch(0, 0, first=True)
            with dve.Fori(0, B // 2 - 1) as pair:
                batch(pair * 2 + 1, 1)
                batch(pair * 2 + 2, 0)
            batch(B - 1, 1, last=True)
            turned_low(B, 0, False)
            finish(B - 1, 0)
            finish(B - 1, 1)

        @block.gpsimd
        def _(pool):
            def prepare():
                pool.memset(ident[:], 0.0).then_inc(const_ready, 1)
                pool.memset(share[:], 1.0 / COUNT).then_inc(const_ready, 1)
                pool.memset(power[:], -0.5).then_inc(const_ready, 1)
                pool.wait_ge(const_ready, 3)
                pool.affine_select(out=ident[:], in_=ident[:], compare_op=ALU.not_equal, fill=1.0, base=0,
                                   pattern=[[-1, P]], channel_multiplier=1).then_inc(const_ready, 1)

            def centre(nb, use):
                pool.wait_ge(stage_read, use + 1)
                f = by_group(front[:, 1, :])
                pool.tensor_tensor(f, f, over_positions(mean[:]), ALU.subtract).then_inc(centred, 1)

            def scale_z(nb, use, blocks=range(KC)):
                pool.wait_ge(stage_read, use + 1)
                pool.tensor_tensor(rstd[:], var_eps[:], power[:], ALU.pow).then_inc(rstd_done, 1)
                pool.wait_ge(rstd_done, nb + 1)
                for k in blocks:
                    f = by_group(front[:, k, :])
                    pool.tensor_tensor(f, f, over_positions(rstd[:]), ALU.mult).then_inc(z_scaled, 1)

            def z_low(nb, z):
                pool.wait_ge(z_hi_done, nb * 2 + 2)
                pool.tensor_tensor(z_lo[:, z, 1, :], front[:, 1, :], z_hi[:, z, 1, :].bitcast(F32),
                                   ALU.subtract).then_inc(z_lo_done1, 1)

            def u_low(b, c):
                n, m = c // 2, c % 2
                at = slice(n * HALF, (n + 1) * HALF)
                pool.wait_ge(u_hi_done, b * 4 + c + 1)
                pool.tensor_tensor(u_lo[:, m, at], u_sum[:, c % 2, :], u_hi[:, m, at].bitcast(F32),
                                   ALU.subtract).then_inc(u_ready, 1)

            def batch(b, z, last=False):
                u_low(b, 2)
                u_low(b, 3)
                if not last:
                    centre(b + 1, stage_use(b, ("mean", 0)))
                    scale_z(b + 1, stage_use(b, ("var", 0)))
                    z_low(b + 1, (z + 1) % 2)
                    u_low(b + 1, 0)
                    u_low(b + 1, 1)

            prepare()
            scale_z(0, 1, [1])
            u_low(0, 0)
            u_low(0, 1)
            batch(0, 0)
            with pool.Fori(0, B // 2 - 1) as pair:
                batch(pair * 2 + 1, 1)
                batch(pair * 2 + 2, 0)
            batch(B - 1, 1, last=True)


def kernel(**inputs):
    import numpy as np
    import concourse.bacc as bacc
    from concourse.bass_utils import run_bass_kernel_spmd

    names = ["x", "L0_conv_Wq", "L0_conv_bq", "L0_conv_Wk", "L0_conv_Wv", "L0_conv_bv", "L0_conv_rel_h", "L0_conv_rel_w"]
    nc = bacc.Bacc("TRN2", target_bir_lowering=False, num_devices=1)
    arrays, args = {}, []
    for name in names:
        a = np.ascontiguousarray(inputs[name])
        arrays[f"in_{name}"] = a
        args.append(nc.dram_tensor(f"in_{name}", a.shape, mybir.dt.from_np(a.dtype), kind="ExternalInput").ap())
    x = inputs["x"]
    args.append(nc.dram_tensor("out", x.shape, mybir.dt.from_np(np.dtype(x.dtype)), kind="ExternalOutput").ap())
    attention_block(nc, *args)
    result = run_bass_kernel_spmd(nc, [arrays], core_ids=[0])
    return result.results[0]["out"]
```

```python
from contextlib import ExitStack

import concourse.bass as bass
from concourse import mybir

F32 = mybir.dt.float32
F32R = mybir.dt.float32r
ALU = mybir.AluOpType
ACT = mybir.ActivationFunctionType
AX = mybir.AxisListType

P = 128
GROUPS = 16
EPS = 1e-5
STEPS = 8
MEAN, VAR = ("mean", 0), ("var", 0)
NEXT = [MEAN, VAR, ("u", 0), ("u", 1)]
MIDDLE = {0: [("u", 2)], 1: [("u", 3), ("v", 0), MEAN], 2: [("v", 1)], 3: [("v", 2), VAR],
          4: [("v", 3)], 5: [("u", 0)], 6: [("u", 1)], 7: []}
AHEAD = [*NEXT, ("v", 0), ("v", 1)]
SLOTS = {"first": {**MIDDLE, 1: [("u", 3), MEAN], 2: [("v", 2)], 3: [VAR]}, "middle": MIDDLE,
         "last": {s: [use for use in uses if use not in NEXT] for s, uses in MIDDLE.items()}}


def in_order(slots, first_turned):
    return [use for s in range(STEPS) for use in [("turn", s, 0), ("turn", s, 1)] * (s >= first_turned) + slots[s]]


USES = {"ahead": AHEAD, "first": in_order(SLOTS["first"], 1), "middle": in_order(MIDDLE, 0),
        "last": in_order(SLOTS["last"], 0), "tail": [("turn", 0, 0), ("turn", 0, 1)]}
PER_BATCH = len(USES["middle"])
BEYOND = len(USES["ahead"]) + len(USES["first"]) - PER_BATCH


def stage_use(b, use, part):
    n = USES[part].index(use)
    if part == "ahead":
        return n
    if part == "first":
        return len(AHEAD) + n
    if part == "tail":
        n -= len(NEXT)
    return b * PER_BATCH + BEYOND + n


def attention_block(nc, x, w_q, b_q, w_k, w_v, b_v, rel_h, rel_w, out):
    B, C, W, H = x.shape
    N = W * H
    KC = C // P
    T = N // P
    HALF = N // 2
    TH = T // 2
    Q = P * 4
    WEIGHT_LOADS = 5 + 2 * KC
    COUNT = C * W * H // GROUPS
    assert KC == 2 and T == STEPS and HALF == Q and B % 2 == 0
    assert PER_BATCH % 2 == 0 and all(len(uses) % 2 == 0 for uses in USES.values())

    x_dram = x.rearrange("b (k p) w h -> b p k (w h)", p=P)
    out_dram = out.rearrange("b (k p) w h -> b p k (w h)", p=P)

    with ExitStack() as ctx:
        def sb(name, shape, dt=F32):
            return ctx.enter_context(nc.sbuf_tensor(name, shape, dt))

        def sem(name):
            return ctx.enter_context(nc.semaphore(name))

        z_hi = sb("z_hi", [P, 2, KC, N], F32R)
        z_lo = sb("z_lo", [P, 2, KC, N], F32R)
        u_hi = sb("u_hi", [P, KC, N], F32R)
        u_lo = sb("u_lo", [P, KC, N], F32R)
        v_hi = sb("v_hi", [P, T, C], F32R)
        v_lo = sb("v_lo", [P, T, C], F32R)
        pt_hi = sb("pt_hi", [P, 2, T, HALF], F32R)
        pt_lo = sb("pt_lo", [P, 2, T, HALF], F32R)
        at_hi = sb("at_hi", [P, KC, C], F32R)
        at_lo = sb("at_lo", [P, KC, C], F32R)
        wvt_hi = sb("wvt_hi", [P, KC, C], F32R)
        wvt_lo = sb("wvt_lo", [P, KC, C], F32R)
        front = sb("front", [P, KC, N])
        squares = sb("squares", [P, KC, N])
        resid = sb("resid", [P, 2, KC, HALF])
        probs = sb("probs", [P, 2, N])
        u_sum = sb("u_sum", [P, 2, HALF])
        r_bias = sb("r_bias", [P, KC, N])
        wq_sb = sb("wq_sb", [P, KC, C])
        wk_sb = sb("wk_sb", [P, KC, C])
        wv_sb = sb("wv_sb", [P, KC, C])
        bq_sb = sb("bq_sb", [P, KC])
        bv_sb = sb("bv_sb", [P, KC])
        rel_sb = sb("rel_sb", [P, KC, H + W])
        relq_sb = sb("relq_sb", [P, KC, H + W])
        relh_kb = sb("relh_kb", [P, KC, H])
        kb_sb = sb("kb_sb", [P, KC])
        ident = sb("ident", [P, P])
        share = sb("share", [P, P])
        power = sb("power", [P, GROUPS])
        part = sb("part", [P, 2, GROUPS])
        mean = sb("mean", [P, GROUPS])
        var_eps = sb("var_eps", [P, GROUPS])
        rstd = sb("rstd", [P, GROUPS])
        neg_max = sb("neg_max", [P, 2])
        row_sum = sb("row_sum", [P, 2])
        row_inv = sb("row_inv", [P, 2])

        scores = [ctx.enter_context(nc.psum_tensor(f"scores{i}", [P, N], F32)) for i in range(2)]
        sums = ctx.enter_context(nc.psum_tensor("sums", [P, KC, HALF], F32))
        stage = [ctx.enter_context(nc.psum_tensor(f"stage{i}", [P, Q], F32)) for i in range(2)]

        weights_in = sem("weights_in")
        x_in = sem("x_in")
        resid_in = [sem(f"resid_in{h}") for h in range(2)]
        stored = [sem(f"stored{h}") for h in range(2)]
        const_ready = sem("const_ready")
        prep_mm = sem("prep_mm")
        prep_hi = sem("prep_hi")
        prep_read = sem("prep_read")
        sum_done = sem("sum_done")
        sumsq_done = sem("sumsq_done")
        stat_mm = sem("stat_mm")
        centred = sem("centred")
        squared = sem("squared")
        rstd_done = sem("rstd_done")
        z_scaled = [sem(f"z_scaled{k}") for k in range(KC)]
        z_hi_done = sem("z_hi_done")
        z_lo_done = [sem(f"z_lo_done{k}") for k in range(KC)]
        u_mm = sem("u_mm")
        u_hi_done = sem("u_hi_done")
        u_ready = sem("u_ready")
        v_mm = sem("v_mm")
        v_hi_done = sem("v_hi_done")
        scores_ready = sem("scores_ready")
        max_done = sem("max_done")
        exp_done = sem("exp_done")
        inv_done = sem("inv_done")
        probs_ready = sem("probs_ready")
        turned = sem("turned")
        pt_hi_done = sem("pt_hi_done")
        pv_done = sem("pv_done")
        out_ready = sem("out_ready")
        stage_read = sem("stage_read")

        def bank_of(use, part):
            return stage[USES[part].index(use) % 2]

        def by_group(ap):
            return ap.rearrange("p (w g r) -> p w g r", g=GROUPS, r=H // GROUPS)

        def over_positions(stat):
            return stat.unsqueeze(1).unsqueeze(3).to_broadcast([P, W, GROUPS, H // GROUPS])

        def whole(ap):
            return ap.rearrange("p k n -> p (k n)")

        def grouped_sum_view(ap):
            return whole(ap).rearrange("p (w g r) -> p g w r", g=GROUPS, r=H // GROUPS)

        block = ctx.enter_context(nc.Block())

        @block.sync
        def _(sp):
            sp.dma_start(front[:], x_dram[0]).then_inc(x_in, 16)
            for h in range(2):
                sp.dma_start(resid[:, h], x_dram[0, :, :, h * HALF:(h + 1) * HALF]).then_inc(resid_in[h], 16)

            def store(b, h):
                sp.wait_ge(out_ready, b * 4 + 2 * h + 2)
                sp.dma_start(out_dram[b, :, :, h * HALF:(h + 1) * HALF], resid[:, h]).then_inc(stored[h], 16)
                sp.wait_ge(stored[h], b * 16 + 16)

            def batch(b, first=False, last=False):
                if not last:
                    for k in range(KC):
                        sp.wait_ge(z_lo_done[k], b + 1)
                    sp.dma_start(front[:], x_dram[b + 1]).then_inc(x_in, 16)
                if not first:
                    for h in range(2):
                        store(b - 1, h)
                        sp.dma_start(resid[:, h], x_dram[b, :, :, h * HALF:(h + 1) * HALF]).then_inc(resid_in[h], 16)

            batch(0, first=True)
            with sp.Fori(0, B // 2 - 1) as pair:
                batch(pair * 2 + 1)
                batch(pair * 2 + 2)
            batch(B - 1, last=True)
            store(B - 1, 0)
            for k in range(KC):
                sp.wait_ge(out_ready, (B - 1) * 4 + KC + k + 1)
                sp.dma_start(out_dram[B - 1, :, k, HALF:], resid[:, 1, k]).then_inc(stored[1], 16)
            sp.wait_ge(stored[1], (B - 1) * 16 + KC * 16)

        @block.tensor
        def _(pe):
            def prepare_a():
                pe.wait_ge(weights_in, 16 * WEIGHT_LOADS)
                for m in range(KC):
                    for k in range(KC):
                        mm = pe.matmul(scores[0][:, m * C:(m + 1) * C], wq_sb[:, k, m * P:(m + 1) * P], wk_sb[:, k, :],
                                       start=(k == 0), stop=(k == KC - 1))
                mm.then_inc(prep_mm, 1)

            def prepare_rest():
                for k in range(KC):
                    for c in range(KC):
                        at = HALF + k * C + c * P
                        mm = pe.transpose(scores[0][:, at:at + P], wv_sb[:, c, k * P:(k + 1) * P], ident[:])
                mm.then_inc(prep_mm, 1)
                for m in range(KC):
                    for k in range(KC):
                        pe.matmul(sums[:, 0, m:m + 1], wk_sb[:, k, m * P:(m + 1) * P], bq_sb[:, k:k + 1],
                                  start=(k == 0), stop=(k == KC - 1))
                for m in range(KC):
                    at = m * (H + W)
                    for k in range(KC):
                        mm = pe.matmul(sums[:, 1, at:at + H + W], wq_sb[:, k, m * P:(m + 1) * P], rel_sb[:, k, :],
                                       start=(k == 0), stop=(k == KC - 1))
                mm.then_inc(prep_mm, 1)

            def stage_bank(use):
                if not isinstance(use, int) or use >= 2:
                    pe.wait_ge(stage_read, use - 1)

            def group_stat(b, nb, which, part_of):
                pe.wait_ge(sumsq_done if which is VAR else sum_done, nb + 1)
                stage_bank(stage_use(b, which, part_of))
                pe.matmul(bank_of(which, part_of)[:, 0:GROUPS], share[:], part[:, int(which is VAR), :],
                          start=True, stop=True).then_inc(stat_mm, 1)

            def u_chunk(b, nb, z, c, part_of):
                n, m = c // 2, c % 2
                stage_bank(stage_use(b, ("u", c), part_of))
                dst = bank_of(("u", c), part_of)
                at = slice(n * HALF, (n + 1) * HALF)
                for k in range(KC):
                    if c == 0:
                        pe.wait_ge(z_lo_done[k], nb + 1)
                    w = slice(m * P, (m + 1) * P)
                    pe.matmul(dst[:], at_hi[:, k, w], z_hi[:, z, k, at], start=(k == 0), stop=False)
                    pe.matmul(dst[:], at_hi[:, k, w], z_lo[:, z, k, at], start=False, stop=False)
                    mm = pe.matmul(dst[:], at_lo[:, k, w], z_hi[:, z, k, at], start=False, stop=(k == KC - 1))
                mm.then_inc(u_mm, 1)

            def v_chunk(b, z, c, part_of):
                stage_bank(stage_use(b, ("v", c), part_of))
                for j in range(2):
                    dst = bank_of(("v", c), part_of)[:, j * C:(j + 1) * C]
                    pos = slice((2 * c + j) * P, (2 * c + j + 1) * P)
                    for k in range(KC):
                        pe.matmul(dst, z_hi[:, z, k, pos], wvt_hi[:, k, :], start=(k == 0), stop=False)
                        pe.matmul(dst, z_hi[:, z, k, pos], wvt_lo[:, k, :], start=False, stop=False)
                        mm = pe.matmul(dst, z_lo[:, z, k, pos], wvt_hi[:, k, :], start=False, stop=(k == KC - 1))
                mm.then_inc(v_mm, 1)

            def score_tile(b, z, s, first):
                if not first or s >= 2:
                    pe.wait_ge(exp_done, b * T + s - 1)
                i = slice(s * P, (s + 1) * P)
                dst = [scores[s % 2][:, n * HALF:(n + 1) * HALF] for n in range(2)]
                for k in range(KC):
                    if s % TH == 0:
                        pe.wait_ge(u_ready, b * 4 + 2 * (s // TH) + k + 1)
                    for w, m in ((u_hi, z_hi), (u_hi, z_lo), (u_lo, z_hi)):
                        for n in range(2):
                            mm = pe.matmul(dst[n], w[:, k, i], m[:, z, k, n * HALF:(n + 1) * HALF],
                                           start=(k == 0 and w is u_hi and m is z_hi), stop=(k == KC - 1 and w is u_lo))
                mm.then_inc(scores_ready, 1)

            def turn_tile(b, s, part_of):
                pe.wait_ge(probs_ready, b * T + s)
                for q in range(2):
                    stage_bank(stage_use(b, ("turn", s, q), part_of))
                    dst = bank_of(("turn", s, q), part_of)
                    for j in range(4):
                        at = (4 * q + j) * P
                        mm = pe.transpose(dst[:, j * P:(j + 1) * P], probs[:, (s + 1) % 2, at:at + P], ident[:])
                    mm.then_inc(turned, 1)

            def value_product(b, s, part_of):
                quarter, h = (s + 3) % 4, 0 if s in (0, 5, 6, 7) else 1
                if s == 5:
                    pe.wait_ge(stage_read, stage_use(b, ("v", 3), part_of) + 1)
                    if part_of != "first":
                        pe.wait_ge(out_ready, b * 4)
                if s == 1:
                    pe.wait_ge(stage_read, stage_use(b, ("turn", 0, 1), part_of) + 1)
                    pe.wait_ge(out_ready, b * 4 - 2)
                for j in range(2 * quarter, 2 * quarter + 2):
                    for c in range(KC):
                        w = slice(c * P, (c + 1) * P)
                        pe.matmul(sums[:, c, :], v_hi[:, j, w], pt_hi[:, h, j, :], start=(j == 0), stop=False)
                        pe.matmul(sums[:, c, :], v_hi[:, j, w], pt_lo[:, h, j, :], start=False, stop=False)
                        mm = pe.matmul(sums[:, c, :], v_lo[:, j, w], pt_hi[:, h, j, :], start=False, stop=(j == T - 1))
                mm.then_inc(pv_done, 1)

            def last_value_product():
                pe.wait_ge(stage_read, stage_use(B, ("turn", 0, 1), "tail") + 1)
                pe.wait_ge(out_ready, B * 4 - 2)
                for c in range(KC):
                    for j in range(T):
                        w = slice(c * P, (c + 1) * P)
                        pe.matmul(sums[:, c, :], v_hi[:, j, w], pt_hi[:, 1, j, :], start=(j == 0), stop=False)
                        pe.matmul(sums[:, c, :], v_hi[:, j, w], pt_lo[:, 1, j, :], start=False, stop=False)
                        mm = pe.matmul(sums[:, c, :], v_lo[:, j, w], pt_hi[:, 1, j, :], start=False, stop=(j == T - 1))
                    mm.then_inc(pv_done, 4 // KC)

            def batch(b, z, part_of="middle"):
                first = part_of == "first"
                for s in range(STEPS):
                    score_tile(b, z, s, first)
                    if not first or s > 0:
                        turn_tile(b, s, part_of)
                    if not first or s >= 5:
                        value_product(b, s, part_of)
                    for kind, c in SLOTS[part_of][s]:
                        if kind == "u":
                            u_chunk(b, b + (c < 2), (z + (c < 2)) % 2, c, part_of)
                        elif kind == "v":
                            v_chunk(b, z, c, part_of)
                        else:
                            group_stat(b, b + 1, MEAN if kind == "mean" else VAR, part_of)

            pe.wait_ge(const_ready, 4)
            group_stat(0, 0, MEAN, "ahead")
            prepare_a()
            group_stat(0, 0, VAR, "ahead")
            prepare_rest()
            pe.wait_ge(prep_read, 2)
            u_chunk(0, 0, 0, 0, "ahead")
            u_chunk(0, 0, 0, 1, "ahead")
            v_chunk(0, 0, 0, "ahead")
            v_chunk(0, 0, 1, "ahead")
            batch(0, 0, "first")
            with pe.Fori(0, B // 2 - 1) as pair:
                batch(pair * 2 + 1, 1)
                batch(pair * 2 + 2, 0)
            batch(B - 1, 1, "last")
            value_product(B, 0, "tail")
            turn_tile(B, 0, "tail")
            last_value_product()

        @block.scalar
        def _(act):
            def prepare():
                for tile, src in ((wq_sb, w_q), (wk_sb, w_k), (wv_sb, w_v)):
                    act.dma_start(tile[:], src.rearrange("(k p) c -> p k c", p=P)).then_inc(weights_in, 16)
                for tile, src in ((bq_sb, b_q), (bv_sb, b_v)):
                    for k in range(KC):
                        act.dma_start(tile[:, k:k + 1], src.rearrange("(k p a) -> k p a", p=P, a=1)[k]).then_inc(weights_in, 16)
                act.dma_start(rel_sb[:, :, 0:H], rel_h.rearrange("a (k p) b h -> p k (a b h)", p=P)).then_inc(weights_in, 16)
                act.dma_start(rel_sb[:, :, H:], rel_w.rearrange("a (k p) w b -> p k (a w b)", p=P)).then_inc(weights_in, 16)
                act.preload_act_table(ACT.Exp)

            def prepare_high():
                for n, dst in enumerate((at_hi, wvt_hi)):
                    act.wait_ge(prep_mm, n + 1)
                    act.activation(whole(dst[:]), scores[0][:, n * HALF:(n + 1) * HALF], ACT.Copy).then_inc(prep_hi, 1)

            def square(nb, prologue=False):
                for k in range(KC):
                    act.wait_ge(centred, k + 1 if prologue else nb * KC + KC)
                    act.activation(squares[:, k], front[:, k], ACT.Square).then_inc(squared, 1)

            def z_high(nb, z, first):
                for k in range(KC):
                    act.wait_ge(z_scaled[k], nb + 1)
                    if k == 0 and not first:
                        act.wait_ge(scores_ready, (nb - 1) * T)
                    act.activation(z_hi[:, z, k, :], front[:, k, :], ACT.Copy).then_inc(z_hi_done, 1)

            def u_high(b, c, use, free):
                n, m = c // 2, c % 2
                act.wait_ge(stage_read, use + 1)
                if free is not None:
                    act.wait_ge(scores_ready, free)
                act.activation(u_hi[:, m, n * HALF:(n + 1) * HALF], u_sum[:, c % 2, :], ACT.Copy).then_inc(u_hi_done, 1)

            def v_high(b, c, part_of):
                act.wait_ge(v_mm, b * 4 + c + 1)
                if part_of not in ("ahead", "first"):
                    act.wait_ge(pv_done, b * 8 - 3 + c)
                act.activation(v_hi[:, 2 * c:2 * c + 2, :].rearrange("p j c -> p (j c)"),
                               bank_of(("v", c), part_of)[:], ACT.Copy).then_inc(v_hi_done, 1)

            def turned_high(b, s, part_of):
                t = (s - 1) % T
                for q in range(2):
                    act.wait_ge(turned, (b * T + s) * 2 - 1 + q)
                    if q == 0 and t % TH == 0 and part_of != "first":
                        act.wait_ge(pv_done, b * 8 - 4 + t)
                    at = slice((t % TH) * P, (t % TH + 1) * P)
                    act.activation(pt_hi[:, t // TH, 4 * q:4 * q + 4, at],
                                   bank_of(("turn", s, q), part_of)[:].rearrange("p (j i) -> p j i", j=4), ACT.Copy).then_inc(pt_hi_done, 1)

            def exponent(b, s, first):
                act.wait_ge(max_done, b * T + s + 1)
                if not first or s >= 2:
                    act.wait_ge(turned, (b * T + s) * 2 - 2)
                act.activation(probs[:, s % 2, :], scores[s % 2][:], ACT.Exp, bias=neg_max[:, s % 2:s % 2 + 1],
                               accum_out=row_sum[:, s % 2:s % 2 + 1]).then_inc(exp_done, 1)

            def batch(b, z, part_of="middle"):
                first, last = part_of == "first", part_of == "last"
                for s in range(STEPS):
                    if not first or s > 0:
                        turned_high(b, s, part_of)
                    exponent(b, s, first)
                    if s == 2 and not last:
                        square(b + 1)
                    for kind, c in SLOTS[part_of][s]:
                        if kind == "u":
                            u_high(b + (c < 2), c, stage_use(b, (kind, c), part_of),
                                   b * T + 4 if c < 2 else None if first else b * T)
                        elif kind == "v":
                            v_high(b, c, part_of)
                    if s == 4 and not last:
                        z_high(b + 1, (z + 1) % 2, first)

            prepare()
            square(0, prologue=True)
            prepare_high()
            z_high(0, 0, True)
            for c in range(2):
                u_high(0, c, stage_use(0, ("u", c), "ahead"), None)
            for c in range(2):
                v_high(0, c, "ahead")
            batch(0, 0, "first")
            with act.Fori(0, B // 2 - 1) as pair:
                batch(pair * 2 + 1, 1)
                batch(pair * 2 + 2, 0)
            batch(B - 1, 1, "last")
            turned_high(B, 0, "tail")

        @block.vector
        def _(dve):
            def prepare_low():
                for n, (hi, lo) in enumerate(((at_hi, at_lo), (wvt_hi, wvt_lo))):
                    dve.wait_ge(prep_hi, n + 1)
                    dve.tensor_tensor(whole(lo[:]), scores[0][:, n * HALF:(n + 1) * HALF], whole(hi[:]).bitcast(F32),
                                      ALU.subtract).then_inc(prep_read, 1)

            def prepare_bias():
                dve.wait_ge(prep_mm, 3)
                dve.tensor_copy(kb_sb[:], sums[:, 0, 0:KC]).then_inc(prep_read, 1)
                dve.tensor_copy(whole(relq_sb[:]), sums[:, 1, 0:KC * (H + W)]).then_inc(prep_read, 1)
                dve.wait_ge(prep_read, 4)
                dve.tensor_tensor(relh_kb[:], relq_sb[:, :, 0:H], kb_sb[:].unsqueeze(2).to_broadcast([P, KC, H]),
                                  ALU.add).then_inc(prep_read, 1)

            def prepare_r(m):
                dve.wait_ge(prep_read, 5)
                dve.tensor_tensor(r_bias[:, m, :].rearrange("p (w h) -> p w h", w=W),
                                  relq_sb[:, m, H:].unsqueeze(2).to_broadcast([P, W, H]),
                                  relh_kb[:, m, :].unsqueeze(1).to_broadcast([P, W, H]), ALU.add).then_inc(prep_read, 1)

            def sum_x(nb):
                dve.wait_ge(x_in, nb * 16 + 16)
                dve.tensor_reduce(part[:, 0, :], grouped_sum_view(front[:]), AX.XY, ALU.add).then_inc(sum_done, 1)

            def sum_squares(nb):
                dve.wait_ge(squared, nb * KC + KC)
                dve.tensor_reduce(part[:, 1, :], grouped_sum_view(squares[:]), AX.XY, ALU.add).then_inc(sumsq_done, 1)

            def read_mean(nb, part_of):
                dve.wait_ge(stat_mm, nb * 2 + 1)
                dve.tensor_copy(mean[:], bank_of(MEAN, part_of)[:, 0:GROUPS]).then_inc(stage_read, 1)

            def centre(nb, k, use):
                dve.wait_ge(stage_read, use + 1)
                f = by_group(front[:, k, :])
                dve.tensor_tensor(f, f, over_positions(mean[:]), ALU.subtract).then_inc(centred, 1)

            def read_var(nb, part_of):
                dve.wait_ge(stat_mm, nb * 2 + 2)
                dve.tensor_scalar(var_eps[:], bank_of(VAR, part_of)[:, 0:GROUPS], EPS, None, ALU.add).then_inc(stage_read, 1)

            def z_low(nb, z, k):
                dve.wait_ge(z_hi_done, nb * KC + k + 1)
                dve.tensor_tensor(z_lo[:, z, k, :], front[:, k, :], z_hi[:, z, k, :].bitcast(F32),
                                  ALU.subtract).then_inc(z_lo_done[k], 1)

            def u_add(b, c, part_of):
                n, m = c // 2, c % 2
                dve.wait_ge(u_mm, b * 4 + c + 1)
                if part_of == "ahead":
                    dve.wait_ge(prep_read, 5 + m + 1)
                else:
                    dve.wait_ge(u_ready, b * 4 + c - 1)
                dve.tensor_tensor(u_sum[:, c % 2, :], bank_of(("u", c), part_of)[:], r_bias[:, m, n * HALF:(n + 1) * HALF],
                                  ALU.add).then_inc(stage_read, 1)

            def u_low_ahead(c):
                dve.wait_ge(u_hi_done, c + 1)
                dve.tensor_tensor(u_lo[:, c, 0:HALF], u_sum[:, c, :], u_hi[:, c, 0:HALF].bitcast(F32),
                                  ALU.subtract).then_inc(u_ready, 1)

            def v_low(b, c, part_of):
                dve.wait_ge(v_hi_done, b * 4 + c + 1)
                at = slice(2 * c, 2 * c + 2)
                dve.tensor_tensor(v_lo[:, at, :].rearrange("p j c -> p (j c)"), bank_of(("v", c), part_of)[:],
                                  v_hi[:, at, :].rearrange("p j c -> p (j c)").bitcast(F32), ALU.subtract).then_inc(stage_read, 1)

            def turned_low(b, s, part_of):
                t = (s - 1) % T
                for q in range(2):
                    at = slice((t % TH) * P, (t % TH + 1) * P)
                    dve.wait_ge(pt_hi_done, (b * T + s) * 2 - 1 + q)
                    dve.tensor_tensor(pt_lo[:, t // TH, 4 * q:4 * q + 4, at],
                                      bank_of(("turn", s, q), part_of)[:].rearrange("p (j i) -> p j i", j=4),
                                      pt_hi[:, t // TH, 4 * q:4 * q + 4, at].bitcast(F32), ALU.subtract).then_inc(stage_read, 1)

            def row_max(b, s):
                dve.wait_ge(scores_ready, b * T + s + 1)
                dve.tensor_reduce(neg_max[:, s % 2:s % 2 + 1], scores[s % 2][:], AX.X, ALU.max, negate=True).then_inc(max_done, 1)

            def normalise(b, s):
                at = slice(s % 2, s % 2 + 1)
                dve.wait_ge(exp_done, b * T + s + 1)
                dve.reciprocal(row_inv[:, at], row_sum[:, at]).then_inc(inv_done, 1)
                dve.wait_ge(inv_done, b * T + s + 1)
                dve.tensor_scalar(probs[:, s % 2, :], probs[:, s % 2, :], row_inv[:, at], None, ALU.mult).then_inc(probs_ready, 1)

            def finish(b, h, last=False):
                dve.wait_ge(resid_in[h], b * 16 + 16)
                for c in range(KC):
                    dve.wait_ge(pv_done, b * 8 + 4 * h + (4 // KC * (c + 1) if last else 4))
                    dve.scalar_tensor_tensor(out=resid[:, h, c, :], in0=sums[:, c, :], scalar=bv_sb[:, c:c + 1],
                                             in1=resid[:, h, c, :], op0=ALU.add, op1=ALU.add).then_inc(out_ready, 1)

            def batch(b, z, part_of="middle"):
                first, last = part_of == "first", part_of == "last"
                for s in range(STEPS):
                    row_max(b, s)
                    if not first or s > 0:
                        turned_low(b, s, part_of)
                    normalise(b, s)
                    if not first and s in (0, 4):
                        finish(b - 1, s // 4)
                    for kind, c in SLOTS[part_of][s]:
                        if kind == "u":
                            u_add(b + (c < 2), c, part_of)
                        elif kind == "v":
                            v_low(b, c, part_of)
                        elif kind == "mean":
                            read_mean(b + 1, part_of)
                        else:
                            read_var(b + 1, part_of)
                    if not last:
                        if s == 0 and not first:
                            sum_x(b + 1)
                        if s == 1:
                            centre(b + 1, 0, stage_use(b, MEAN, part_of))
                        if s == 2:
                            sum_squares(b + 1)
                        if s == 4:
                            z_low(b + 1, (z + 1) % 2, 0)

            sum_x(0)
            read_mean(0, "ahead")
            for k in range(KC):
                centre(0, k, stage_use(0, MEAN, "ahead"))
            sum_squares(0)
            read_var(0, "ahead")
            prepare_low()
            dve.wait_ge(rstd_done, 1)
            f0 = by_group(front[:, 0, :])
            dve.tensor_tensor(f0, f0, over_positions(rstd[:]), ALU.mult).then_inc(z_scaled[0], 1)
            prepare_bias()
            z_low(0, 0, 0)
            z_low(0, 0, 1)
            for c in range(2):
                prepare_r(c)
                u_add(0, c, "ahead")
                u_low_ahead(c)
            v_low(0, 0, "ahead")
            sum_x(1)
            v_low(0, 1, "ahead")
            batch(0, 0, "first")
            with dve.Fori(0, B // 2 - 1) as pair:
                batch(pair * 2 + 1, 1)
                batch(pair * 2 + 2, 0)
            batch(B - 1, 1, "last")
            finish(B - 1, 0)
            turned_low(B, 0, "tail")
            finish(B - 1, 1, last=True)

        @block.gpsimd
        def _(pool):
            def prepare():
                pool.memset(ident[:], 0.0).then_inc(const_ready, 1)
                pool.memset(share[:], 1.0 / COUNT).then_inc(const_ready, 1)
                pool.memset(power[:], -0.5).then_inc(const_ready, 1)
                pool.wait_ge(const_ready, 3)
                pool.affine_select(out=ident[:], in_=ident[:], compare_op=ALU.not_equal, fill=1.0, base=0,
                                   pattern=[[-1, P]], channel_multiplier=1).then_inc(const_ready, 1)

            def centre(nb, use):
                pool.wait_ge(stage_read, use + 1)
                f = by_group(front[:, 1, :])
                pool.tensor_tensor(f, f, over_positions(mean[:]), ALU.subtract).then_inc(centred, 1)

            def scale_z(nb, use, blocks=range(KC)):
                pool.wait_ge(stage_read, use + 1)
                pool.tensor_tensor(rstd[:], var_eps[:], power[:], ALU.pow).then_inc(rstd_done, 1)
                pool.wait_ge(rstd_done, nb + 1)
                for k in blocks:
                    f = by_group(front[:, k, :])
                    pool.tensor_tensor(f, f, over_positions(rstd[:]), ALU.mult).then_inc(z_scaled[k], 1)

            def z_low(nb, z):
                pool.wait_ge(z_hi_done, nb * 2 + 2)
                pool.tensor_tensor(z_lo[:, z, 1, :], front[:, 1, :], z_hi[:, z, 1, :].bitcast(F32),
                                   ALU.subtract).then_inc(z_lo_done[1], 1)

            def u_low(b, c):
                n, m = c // 2, c % 2
                at = slice(n * HALF, (n + 1) * HALF)
                pool.wait_ge(u_hi_done, b * 4 + c + 1)
                pool.tensor_tensor(u_lo[:, m, at], u_sum[:, c % 2, :], u_hi[:, m, at].bitcast(F32),
                                   ALU.subtract).then_inc(u_ready, 1)

            def batch(b, z, part_of="middle"):
                u_low(b, 2)
                u_low(b, 3)
                if part_of != "last":
                    centre(b + 1, stage_use(b, MEAN, part_of))
                    scale_z(b + 1, stage_use(b, VAR, part_of))
                    z_low(b + 1, (z + 1) % 2)
                    u_low(b + 1, 0)
                    u_low(b + 1, 1)

            prepare()
            scale_z(0, stage_use(0, VAR, "ahead"), [1])
            batch(0, 0, "first")
            with pool.Fori(0, B // 2 - 1) as pair:
                batch(pair * 2 + 1, 1)
                batch(pair * 2 + 2, 0)
            batch(B - 1, 1, "last")


def kernel(**inputs):
    import numpy as np
    import concourse.bacc as bacc
    from concourse.bass_utils import run_bass_kernel_spmd

    names = ["x", "L0_conv_Wq", "L0_conv_bq", "L0_conv_Wk", "L0_conv_Wv", "L0_conv_bv", "L0_conv_rel_h", "L0_conv_rel_w"]
    nc = bacc.Bacc("TRN2", target_bir_lowering=False, num_devices=1)
    arrays, args = {}, []
    for name in names:
        a = np.ascontiguousarray(inputs[name])
        arrays[f"in_{name}"] = a
        args.append(nc.dram_tensor(f"in_{name}", a.shape, mybir.dt.from_np(a.dtype), kind="ExternalInput").ap())
    x = inputs["x"]
    args.append(nc.dram_tensor("out", x.shape, mybir.dt.from_np(np.dtype(x.dtype)), kind="ExternalOutput").ap())
    attention_block(nc, *args)
    result = run_bass_kernel_spmd(nc, [arrays], core_ids=[0])
    return result.results[0]["out"]
```
